# Optimizing a Trainium2 kernel written in Bass

```python
import numpy as np
import jax
import jax.numpy as jnp

def _softmax(x, axis=-1):
    return jax.nn.softmax(x, axis=axis)

def _gelu(x):
    return jax.nn.gelu(x, approximate=True)

def _silu(x):
    return jax.nn.silu(x)

def _sigmoid(x):
    return jax.nn.sigmoid(x)

def _layernorm(x, axis=-1, eps=1e-05):
    m = jnp.mean(x, axis=axis, keepdims=True)
    v = jnp.var(x, axis=axis, keepdims=True)
    return (x - m) / jnp.sqrt(v + eps)

def _scatter_add(tgt, idx, src, axis=0):
    return tgt.at[idx].add(src)

def _segment_sum(src, seg, n):
    return jax.ops.segment_sum(src, seg, n)
kernel_name = 'mk_decoder_preln_d1_seqx_r4_c810b8'

def setup_inputs(seed: int=0):
    np.random.seed(seed)
    _w = jnp.asarray

    def _rec_inputs():
        import jax
        import jax.numpy as jnp
        _rk = jax.random.key(seed)
        x = 7.22e-05 + 1 * jax.random.normal(jax.random.fold_in(_rk, 1), (4, 512, 512), jnp.float32)
        _lenS = 512 - jax.random.randint(jax.random.fold_in(_rk, 7), (4,), 0, max(1, 512 // 4) + 1, jnp.int32)
        _lenS2 = 512 - jax.random.randint(jax.random.fold_in(_rk, 8), (4,), 0, max(1, 512 // 4) + 1, jnp.int32)
        _ctx_512P = jax.random.normal(jax.random.fold_in(_rk, 11), (4, 16, 128), jnp.float32)
        _ctx_512c = jax.random.dirichlet(jax.random.fold_in(_rk, 511), 0.3 * jnp.ones((16,), jnp.float32), (4, 512))
        _ctx_512t = jnp.einsum('bsk,bkd->bsd', _ctx_512c, _ctx_512P)
        _ctx_512t = _ctx_512t * jax.lax.rsqrt(jnp.mean(jnp.square(_ctx_512t)) + 1e-12) * 0.953939
        ctx_512 = -0.000514642 + 1.00011 * (_ctx_512t + 0.3 * jax.random.normal(jax.random.fold_in(_rk, 611), (4, 512, 128), jnp.float32))
        return (x, ctx_512)
    x, ctx_512 = _rec_inputs()

    def _L0_attn_setup():
        import jax, jax.numpy as jnp
        import numpy as np
        D_MODEL = 512
        D_STATE = 16
        D_CONV = 4
        EXPAND = 2
        H = 16
        D_INNER = D_MODEL * EXPAND
        D_HEAD = D_INNER // H
        TOTAL = 2 * D_INNER + H + 2 * H * D_STATE
        BATCH = 4
        SEQ = 1024
        EPS = 1.1920929e-07

        def _forward(x, w_norm, W_in, w_conv, dt_bias, A_log, W_h2i, W_out):
            b, l, _ = x.shape
            residual = x
            xn = x * jax.lax.rsqrt(jnp.mean(x * x, axis=-1, keepdims=True) + EPS) * w_norm
            proj = jnp.einsum('bld,td->blt', xn, W_in)
            z = proj[..., :D_INNER]
            xi = proj[..., D_INNER:2 * D_INNER]
            dt = proj[..., 2 * D_INNER:2 * D_INNER + H]
            o = 2 * D_INNER + H
            Bm = proj[..., o:o + H * D_STATE].reshape(b, l, H, D_STATE)
            Cm = proj[..., o + H * D_STATE:].reshape(b, l, H, D_STATE)
            xc = jax.lax.conv_general_dilated(xi.transpose(0, 2, 1), w_conv, window_strides=(1,), padding=[(D_CONV - 1, 0)], feature_group_count=D_INNER)
            xi = jax.nn.silu(xc.transpose(0, 2, 1))
            dt = jax.nn.softplus(dt + dt_bias)
            A = -jnp.exp(A_log)
            dA = jnp.exp(dt * A)
            x_mean = xi.reshape(b, l, H, D_HEAD).mean(axis=-1)
            u = (dt * x_mean)[..., None] * Bm
            h0 = jnp.zeros((b, H, D_STATE), xi.dtype)

            def step(h, inp):
                dA_t, u_t, C_t = inp
                h = dA_t[..., None] * h + u_t
                y_t = jnp.sum(h * C_t, axis=-1)
                return (h, y_t)
            _, ys = jax.lax.scan(step, h0, (dA.transpose(1, 0, 2), u.transpose(1, 0, 2, 3), Cm.transpose(1, 0, 2, 3)))
            y = ys.transpose(1, 0, 2)
            y = jnp.einsum('blh,ih->bli', y, W_h2i)
            y = y * jax.nn.silu(z)
            out = jnp.einsum('bli,di->bld', y, W_out) + residual
            return out
        key = jax.random.key(seed)
        ks = jax.random.split(key, 6)
        s = 0.02
        return {'x': jax.random.normal(ks[0], (BATCH, SEQ, D_MODEL), jnp.float32), 'w_norm': jnp.ones((D_MODEL,), jnp.float32), 'W_in': jax.random.normal(ks[1], (TOTAL, D_MODEL), jnp.float32) * s, 'w_conv': jax.random.normal(ks[2], (D_INNER, 1, D_CONV), jnp.float32) * 0.2, 'dt_bias': jax.random.normal(ks[3], (H,), jnp.float32), 'A_log': jnp.log(0.001 + jnp.arange(1, H + 1, dtype=jnp.float32)), 'W_h2i': jax.random.normal(ks[4], (D_INNER, H), jnp.float32) * s, 'W_out': jax.random.normal(ks[5], (D_MODEL, D_INNER), jnp.float32) * s}
    _L0_attn_all = _L0_attn_setup()
    _L0_attn_in = {k: v for k, v in _L0_attn_all.items() if k in ('w_norm', 'W_in', 'w_conv', 'dt_bias', 'A_log', 'W_h2i', 'W_out')}
    del _L0_attn_all

    def _L0_xattn_setup():
        import jax, jax.numpy as jnp
        import numpy as np
        import math
        NUM_Q_HEADS = 32
        NUM_KV_HEADS = 8
        key = jax.random.key(seed)
        k1, k2, k3 = jax.random.split(key, 3)
        B, S, E = (2, 512, 512)
        kv_E = NUM_KV_HEADS * (E // NUM_Q_HEADS)
        q = jax.random.normal(k1, (B, S, E), dtype=jnp.float32)
        k = jax.random.normal(k2, (B, S, kv_E), dtype=jnp.float32)
        v = jax.random.normal(k3, (B, S, kv_E), dtype=jnp.float32)
        return {'q': q, 'k': k, 'v': v}
    _L0_xattn_all = _L0_xattn_setup()
    _L0_xattn_in = {k: v for k, v in _L0_xattn_all.items() if k in ()}
    del _L0_xattn_all

    def _L0_ffn_setup():
        import jax, jax.numpy as jnp
        import numpy as np
        B, S, H = (1, 256, 512)
        F = 256
        E = 16
        K = 2
        NS = 1
        ROUTE_SCALE = 1.0
        key = jax.random.key(seed)
        ks = jax.random.split(key, 8)

        def w(k, shape, fan_in):
            return jax.random.normal(k, shape, jnp.float32) * fan_in ** (-0.5)
        return {'hidden_states': jax.random.normal(ks[0], (B, S, H), jnp.float32), 'gate_w': w(ks[1], (H, E), H), 'expert_bias': jnp.zeros((E,), jnp.float32), 'shared_gate_w': w(ks[2], (H, F * NS), H), 'shared_up_w': w(ks[3], (H, F * NS), H), 'shared_down_w': w(ks[4], (F * NS, H), F * NS), 'experts_gate_up': w(ks[5], (E, H, 2 * F), H), 'experts_down': w(ks[6], (E, F, H), F)}
    _L0_ffn_all = _L0_ffn_setup()
    _L0_ffn_in = {k: v for k, v in _L0_ffn_all.items() if k in ('gate_w', 'expert_bias', 'shared_gate_w', 'shared_up_w', 'shared_down_w', 'experts_gate_up', 'experts_down')}
    del _L0_ffn_all
    return {'x': x, 'ctx_512': ctx_512, 'L0_attn_w_norm': _L0_attn_in['w_norm'], 'L0_attn_W_in': _L0_attn_in['W_in'], 'L0_attn_w_conv': _L0_attn_in['w_conv'], 'L0_attn_dt_bias': _L0_attn_in['dt_bias'], 'L0_attn_A_log': _L0_attn_in['A_log'], 'L0_attn_W_h2i': _L0_attn_in['W_h2i'], 'L0_attn_W_out': _L0_attn_in['W_out'], 'L0_ffn_gate_w': _L0_ffn_in['gate_w'], 'L0_ffn_expert_bias': _L0_ffn_in['expert_bias'], 'L0_ffn_shared_gate_w': _L0_ffn_in['shared_gate_w'], 'L0_ffn_shared_up_w': _L0_ffn_in['shared_up_w'], 'L0_ffn_shared_down_w': _L0_ffn_in['shared_down_w'], 'L0_ffn_experts_gate_up': _L0_ffn_in['experts_gate_up'], 'L0_ffn_experts_down': _L0_ffn_in['experts_down']}

def reference(x, ctx_512, L0_attn_w_norm, L0_attn_W_in, L0_attn_w_conv, L0_attn_dt_bias, L0_attn_A_log, L0_attn_W_h2i, L0_attn_W_out, L0_ffn_gate_w, L0_ffn_expert_bias, L0_ffn_shared_gate_w, L0_ffn_shared_up_w, L0_ffn_shared_down_w, L0_ffn_experts_gate_up, L0_ffn_experts_down):
    import jax
    import jax.numpy as jnp

    def _L0_attn_ref(x, w_norm, W_in, w_conv, dt_bias, A_log, W_h2i, W_out):
        import jax, jax.numpy as jnp
        import numpy as np
        D_MODEL = 512
        D_STATE = 16
        D_CONV = 4
        EXPAND = 2
        H = 16
        D_INNER = D_MODEL * EXPAND
        D_HEAD = D_INNER // H
        TOTAL = 2 * D_INNER + H + 2 * H * D_STATE
        BATCH = 4
        SEQ = 1024
        EPS = 1.1920929e-07

        def _forward(x, w_norm, W_in, w_conv, dt_bias, A_log, W_h2i, W_out):
            b, l, _ = x.shape
            residual = x
            xn = x * jax.lax.rsqrt(jnp.mean(x * x, axis=-1, keepdims=True) + EPS) * w_norm
            proj = jnp.einsum('bld,td->blt', xn, W_in)
            z = proj[..., :D_INNER]
            xi = proj[..., D_INNER:2 * D_INNER]
            dt = proj[..., 2 * D_INNER:2 * D_INNER + H]
            o = 2 * D_INNER + H
            Bm = proj[..., o:o + H * D_STATE].reshape(b, l, H, D_STATE)
            Cm = proj[..., o + H * D_STATE:].reshape(b, l, H, D_STATE)
            xc = jax.lax.conv_general_dilated(xi.transpose(0, 2, 1), w_conv, window_strides=(1,), padding=[(D_CONV - 1, 0)], feature_group_count=D_INNER)
            xi = jax.nn.silu(xc.transpose(0, 2, 1))
            dt = jax.nn.softplus(dt + dt_bias)
            A = -jnp.exp(A_log)
            dA = jnp.exp(dt * A)
            x_mean = xi.reshape(b, l, H, D_HEAD).mean(axis=-1)
            u = (dt * x_mean)[..., None] * Bm
            h0 = jnp.zeros((b, H, D_STATE), xi.dtype)

            def step(h, inp):
                dA_t, u_t, C_t = inp
                h = dA_t[..., None] * h + u_t
                y_t = jnp.sum(h * C_t, axis=-1)
                return (h, y_t)
            _, ys = jax.lax.scan(step, h0, (dA.transpose(1, 0, 2), u.transpose(1, 0, 2, 3), Cm.transpose(1, 0, 2, 3)))
            y = ys.transpose(1, 0, 2)
            y = jnp.einsum('blh,ih->bli', y, W_h2i)
            y = y * jax.nn.silu(z)
            out = jnp.einsum('bli,di->bld', y, W_out) + residual
            return out
        return _forward(x, w_norm, W_in, w_conv, dt_bias, A_log, W_h2i, W_out)

    def _L0_xattn_ref(q, k, v):
        import jax, jax.numpy as jnp
        import numpy as np
        import math
        NUM_Q_HEADS = 32
        NUM_KV_HEADS = 8
        B, S, E = q.shape
        H, KV = (NUM_Q_HEADS, NUM_KV_HEADS)
        D = E // H
        G = H // KV
        scale = math.sqrt(D)
        qh = q.reshape(B, S, KV, G, D).transpose(0, 2, 3, 1, 4)
        kh = k.reshape(B, S, KV, D).transpose(0, 2, 1, 3)
        vh = v.reshape(B, S, KV, D).transpose(0, 2, 1, 3)
        scores = jnp.einsum('bkgsd,bktd->bkgst', qh, kh) / scale
        weights = jax.nn.softmax(scores, axis=-1)
        out = jnp.einsum('bkgst,bktd->bkgsd', weights, vh)
        return out.transpose(0, 3, 1, 2, 4).reshape(B, S, E)

    def _L0_ffn_ref(hidden_states, gate_w, expert_bias, shared_gate_w, shared_up_w, shared_down_w, experts_gate_up, experts_down):
        import jax, jax.numpy as jnp
        import numpy as np
        B, S, H = (1, 256, 512)
        F = 256
        E = 16
        K = 2
        NS = 1
        ROUTE_SCALE = 1.0
        b, s, h = hidden_states.shape
        x = hidden_states.reshape(-1, h)
        T = x.shape[0]
        router_logits = (x @ gate_w).astype(jnp.float32)
        scores = jax.nn.sigmoid(router_logits)
        _, selected = jax.lax.top_k(scores + expert_bias[None, :], K)
        top_scores = jnp.take_along_axis(scores, selected, axis=1)
        top_scores = top_scores / (top_scores.sum(-1, keepdims=True) + 1e-20)
        top_scores = top_scores * ROUTE_SCALE
        shared = jax.nn.silu(x @ shared_gate_w) * (x @ shared_up_w) @ shared_down_w
        comb = jnp.zeros((T, E), jnp.float32).at[jnp.arange(T)[:, None], selected].add(top_scores)
        routed = jnp.zeros_like(x)
        for e in range(E):
            gu = x @ experts_gate_up[e]
            g, u = jnp.split(gu, 2, axis=-1)
            routed = routed + comb[:, e:e + 1] * (jax.nn.silu(g) * u @ experts_down[e])
        return (shared + routed).reshape(b, s, h)
    x = x + _L0_attn_ref(_layernorm(x, axis=-1), L0_attn_w_norm, L0_attn_W_in, L0_attn_w_conv, L0_attn_dt_bias, L0_attn_A_log, L0_attn_W_h2i, L0_attn_W_out)
    x = x + _L0_xattn_ref(_layernorm(x, axis=-1), ctx_512, ctx_512)
    x = x + _L0_ffn_ref(_layernorm(x, axis=-1), L0_ffn_gate_w, L0_ffn_expert_bias, L0_ffn_shared_gate_w, L0_ffn_shared_up_w, L0_ffn_shared_down_w, L0_ffn_experts_gate_up, L0_ffn_experts_down)
    return x

_drawn_inputs = setup_inputs


def setup_inputs(seed=0):
    import zlib

    import numpy as np

    out = dict(_drawn_inputs(seed))
    spreads = {'L0_attn_w_norm': (1.0, 0.2), 'L0_ffn_expert_bias': (0.0, 0.1)}
    factors = {}
    for name, (base, spread) in spreads.items():
        noise = np.random.default_rng([zlib.crc32(name.encode()), seed]).standard_normal(out[name].shape)
        drawn = base * np.exp(spread * noise) if base else spread * noise
        out[name] = jnp.asarray(drawn.astype(out[name].dtype))
    for name, factor in factors.items():
        out[name] = (out[name] * factor).astype(out[name].dtype)
    return out
```

```python
from contextlib import ExitStack

import numpy as np

import concourse.bass as bass
from concourse import mybir

F32 = mybir.dt.float32
BF16 = mybir.dt.bfloat16
ALU = mybir.AluOpType
ACT = mybir.ActivationFunctionType
AX = mybir.AxisListType

P = 128
LN_EPS = 1e-5
RMS_EPS = 1.1920929e-07


def alone(engine):
    engine.nop(nofuse=True)


class Steps:

    def __init__(self, engine, sem, base=0):
        self.engine, self.sem, self.base, self.n = engine, sem, base, 0

    def then(self, instruction):
        self.n += 1
        instruction.then_inc(self.sem, 1)
        self.engine.wait_ge(self.sem, self.base + self.n)


def mixer_phase(nc, dram, x1, ident, identb, batches):
    SEQ = 512
    TB = SEQ // P
    D = 512
    KD = D // P
    w_in, w_out, w_h2i, conv = dram["w_in"], dram["w_out"], dram["w_h2i"], dram["conv"]
    INNER = w_out.shape[1] * P
    KI = INNER // P
    H = 16
    NS = 2
    O_XI, O_DT, O_B = INNER, 2 * INNER, 2 * INNER + H
    O_C = O_B + NS * P

    with ExitStack() as ctx:
        sb = lambda name, shape, dt=F32: ctx.enter_context(nc.sbuf_tensor(name, shape, dt))
        ps = lambda name: ctx.enter_context(nc.psum_tensor(name, [P, SEQ], F32))
        sem = lambda name: ctx.enter_context(nc.semaphore(name))

        win = sb("win", [P, KD, O_C + NS * P])
        wout = sb("wout", [P, KI, D])
        wh2i = sb("wh2i", [H, INNER])
        convw = sb("convw", [P, KI, 4])
        wnorm = sb("wnorm", [P, KD, 1])
        dtb = sb("dtb", [H, 1])
        alog = sb("alog", [H, 1])
        neg_a = sb("neg_a", [H, 1])
        head_mean = sb("head_mean", [P, KI, H])
        spread = sb("spread", [H, NS, P])
        state_sum = sb("state_sum", [P, NS, H])
        xt = sb("xt", [P, TB, D])
        hln = sb("hln", [P, TB, D])
        hn = sb("hn", [P, TB, D])
        xnT = sb("xnT", [P, KD, SEQ])
        st = sb("st", [P, TB, 6])
        mv = sb("mv", [P, TB, 2])
        var_eps = sb("var_eps", [P, TB, 2])
        std = sb("std", [P, TB, 2])
        rstd = sb("rstd", [P, TB, 2])
        dtx = sb("dtx", [H, SEQ])
        dta = sb("dta", [H, SEQ])
        dte = sb("dte", [H, SEQ])
        dtu = sb("dtu", [H, SEQ])
        dtl = sb("dtl", [H, SEQ])
        dtr = sb("dtr", [H, SEQ])
        dt = sb("dt", [H, SEQ])
        decay = sb("decay", [H, SEQ])
        gain = sb("gain", [H, SEQ])
        bsb = sb("bsb", [P, NS, SEQ])
        csb = sb("csb", [P, NS, SEQ])
        u = sb("u", [P, NS, SEQ])
        state = sb("state", [P, NS, SEQ])
        hc = sb("hc", [P, NS, SEQ])
        xa = sb("xa", [P, 3, SEQ])
        xs = sb("xs", [P, 2, SEQ])
        zs = sb("zs", [P, KI, SEQ])
        ysb = sb("ysb", [H, SEQ])

        acc = [ps(f"acc{i}") for i in range(4)]
        ps_mean, ps_decay, ps_gain, ps_y = ps("ps_mean"), ps("ps_decay"), ps("ps_gain"), ps("ps_y")
        tbank = [ps_y, ps_gain]

        s_w_in = [sem(f"w_in_loaded{i}") for i in range(3)]
        s_w_rest, s_const, s_x = sem("w_rest_loaded"), sem("const_loaded"), sem("x_loaded")
        s_hln, s_xr = sem("ln_done"), sem("residual_stored")
        s_ve, s_std = sem("variance_ready"), sem("std_ready")
        s_tr, s_xnT = sem("tokens_transposed"), sem("xnT_ready")
        s_dt_mm, s_bc_mm, s_xi_mm, s_z_mm = sem("dt_mm"), sem("bc_mm"), sem("xi_mm"), sem("z_mm")
        s_h2i_mm, s_out_mm = sem("h2i_mm"), sem("out_mm")
        s_dt_abs, s_dt_exp, s_dt_u, s_dt_ln = sem("dt_abs"), sem("dt_exp"), sem("dt_u"), sem("dt_ln")
        s_dt, s_decay, s_gain = sem("dt_ready"), sem("decay_ready"), sem("gain_ready")
        s_bc, s_tap, s_conv, s_silu = sem("bc_copied"), sem("first_tap"), sem("conv_done"), sem("xi_silu")
        s_xs_read, s_z, s_spread, s_scan = sem("xs_read"), sem("z_silu"), sem("spread_mm"), sem("scan_done")
        s_hc, s_y_mm, s_y, s_gated, s_x1 = sem("hc_ready"), sem("y_mm"), sem("y_copied"), sem("gated"), sem("x1_ready")
        zero = sb("zero", [P, 1, D])
        s_zero, s_list = sem("zero_set"), sem("list_zeroed")
        s_nega, s_v = sem("neg_a_ready"), sem("vector_steps")

        block = ctx.enter_context(nc.Block())

        @block.sync
        def _(sp):
            xd = dram["x"]

            def load_x(b):
                sp.dma_start(xt[:, :, :], xd[b * TB:(b + 1) * TB].rearrange("t p d -> p t d")
                             if isinstance(b, int) else xd[bass.ds(b * TB, TB)].rearrange("t p d -> p t d")
                             ).then_inc(s_x, 16)

            load_x(0)
            sp.dma_start(ident[:, :], dram["ident"]).then_inc(s_const, 16)
            sp.dma_start(identb[:, :], dram["identb"]).then_inc(s_w_rest, 16)
            sp.dma_start(wnorm[:, :, 0], dram["w_norm"]).then_inc(s_const, 16)
            sp.dma_start(dtb[:, :], dram["dt_bias"]).then_inc(s_const, 16)
            sp.dma_start(alog[:, :], dram["a_log"]).then_inc(s_const, 16)
            sp.dma_start(convw[:, :, :], conv).then_inc(s_const, 16)
            sp.dma_start(win[:, :, O_DT:], w_in[:, :, O_DT:]).then_inc(s_w_in[0], 16)
            sp.dma_start(win[:, :, O_XI:O_DT], w_in[:, :, O_XI:O_DT]).then_inc(s_w_in[1], 16)
            sp.dma_start(head_mean[:, :, :], dram["head_mean"]).then_inc(s_w_rest, 16)
            sp.dma_start(win[:, :, :O_XI], w_in[:, :, :O_XI]).then_inc(s_w_in[2], 16)
            sp.dma_start(spread[:, :, :], dram["spread"]).then_inc(s_w_rest, 16)
            sp.dma_start(state_sum[:, :, :], dram["state_sum"]).then_inc(s_w_rest, 16)
            sp.dma_start(wh2i[:, :], w_h2i).then_inc(s_w_rest, 16)
            sp.dma_start(wout[:, :, :], w_out).then_inc(s_w_rest, 16)
            sp.wait_ge(s_zero, 1)
            sp.dma_start(dram["list_x"].rearrange("(n p) d -> p n d", p=P),
                         zero[:, :, :].to_broadcast([P, dram["list_x"].shape[0] // P, D])).then_inc(s_list, 16)
            with sp.Fori(0, batches - 1) as b:
                sp.wait_ge(s_hln, b + 1)
                sp.wait_ge(s_xr, b + 1)
                alone(sp)
                load_x(b + 1)
            sp.wait_ge(s_list, 16)

        @block.gpsimd
        def _(pool):
            nc.gpsimd.memset(zero[:, :, :], 0.0).then_inc(s_zero, 1)

            def residual(b):
                pool.wait_ge(s_hln, b + 1)
                nc.gpsimd.tensor_tensor(x1[:, bass.ds(b * TB, TB), :], xt[:, :, :], hln[:, :, :],
                                        ALU.add).then_inc(s_xr, 1)

            with pool.Fori(0, batches) as b:
                residual(b)

        @block.vector
        def _(dve):
            def layer_norm(b, steps):
                dve.wait_ge(s_x, 16 * (b + 1))
                for j in range(TB):
                    ins = nc.vector.bn_stats(st[:, j, :], xt[:, j, :])
                steps.then(ins)
                alone(dve)
                for j in range(TB):
                    ins = nc.vector.bn_aggr(mv[:, j, :], st[:, j, :])
                steps.then(ins)
                steps.then(nc.vector.tensor_scalar(var_eps[:, :, 0], mv[:, :, 1], LN_EPS, None, ALU.add))
                nc.vector.scalar_tensor_tensor(out=var_eps[:, :, 1], in0=var_eps[:, :, 0], scalar=RMS_EPS,
                                               in1=mv[:, :, 1], op0=ALU.mult, op1=ALU.add).then_inc(s_ve, 1)
                dve.wait_ge(s_std, b + 1)
                steps.then(nc.vector.reciprocal(rstd[:, :, :], std[:, :, :]))
                dve.wait_ge(s_tr, TB * b)
                dve.wait_ge(s_xr, b)
                for j in range(TB):
                    nc.vector.tensor_scalar(hn[:, j, :], xt[:, j, :], mv[:, j, 0:1], rstd[:, j, 1:2],
                                            ALU.subtract, ALU.mult)
                for j in range(TB):
                    last = nc.vector.tensor_scalar(hln[:, j, :], xt[:, j, :], mv[:, j, 0:1], rstd[:, j, 0:1],
                                                   ALU.subtract, ALU.mult)
                last.then_inc(s_hln, 1)

            def evacuate_transposes(b):
                for j in range(TB):
                    dve.wait_ge(s_tr, TB * b + j + 1)
                    nc.vector.tensor_tensor(xnT[:, :, j * P:(j + 1) * P],
                                            tbank[j % 2][:, :].rearrange("p (k t) -> p k t", k=KD),
                                            wnorm[:, :, :].to_broadcast([P, KD, P]), ALU.mult).then_inc(s_xnT, 1)

            def mixer(b, more):
                steps = Steps(dve, s_v, LN0 + b * PER)
                dve.wait_ge(s_dt_mm, b + 1)
                steps.then(nc.vector.tensor_scalar(dtx[:, :], acc[0][0:H, :], dtb[:, 0:1], None, ALU.add))
                steps.then(nc.vector.tensor_scalar(dta[:, :], dtx[:, :], -1.0, None, ALU.mult))
                nc.vector.tensor_tensor(dta[:, :], dta[:, :], dtx[:, :], ALU.min).then_inc(s_dt_abs, 1)
                dve.wait_ge(s_dt_exp, b + 1)
                nc.vector.tensor_scalar(dtu[:, :], dte[:, :], 1.0, None, ALU.add).then_inc(s_dt_u, 1)
                dve.wait_ge(s_dt_u, b + 1)
                steps.then(nc.vector.scalar_tensor_tensor(out=dte[:, :], in0=dtu[:, :], scalar=1.0, in1=dte[:, :],
                                                          op0=ALU.subtract, op1=ALU.subtract))
                steps.then(nc.vector.reciprocal(dtr[:, :], dtu[:, :]))
                steps.then(nc.vector.tensor_tensor(dtr[:, :], dte[:, :], dtr[:, :], ALU.mult))
                steps.then(nc.vector.scalar_tensor_tensor(out=dtx[:, :], in0=dtx[:, :], scalar=0.0, in1=dtr[:, :],
                                                          op0=ALU.max, op1=ALU.subtract))
                dve.wait_ge(s_dt_ln, b + 1)
                nc.vector.tensor_tensor(dt[:, :], dtx[:, :], dtl[:, :], ALU.add).then_inc(s_dt, 1)

                for i in range(KI):
                    dve.wait_ge(s_tap, KI * b + i + 1)
                    for tap in (1, 2, 3):
                        ins = nc.vector.scalar_tensor_tensor(
                            out=xa[:, i % 3, tap:], in0=acc[(5 + i) % 4][:, :SEQ - tap],
                            scalar=convw[:, i, 3 - tap:4 - tap], in1=xa[:, i % 3, tap:],
                            op0=ALU.mult, op1=ALU.add)
                        if tap == 3:
                            ins.then_inc(s_conv, 1)
                        else:
                            steps.then(ins)
                dve.wait_ge(s_xs_read, KI * (b + 1))
                dve.wait_ge(s_dt, b + 1)
                nc.vector.tensor_tensor(gain[:, :], ps_mean[0:H, :], dt[:, :], ALU.mult).then_inc(s_gain, 1)
                for k in range(NS):
                    dve.wait_ge(s_spread, NS * b + k + 1)
                    dve.wait_ge(s_bc, 4 * (b + 1))
                    steps.then(nc.vector.tensor_tensor(u[:, k, :], ps_gain[:, :], bsb[:, k, :], ALU.mult))
                    nc.vector.tensor_tensor_scan(state[:, k, :], ps_decay[:, :], u[:, k, :], 0.0,
                                                 ALU.mult, ALU.add).then_inc(s_scan, 1)
                    dve.wait_ge(s_scan, NS * b + k + 1)
                    dve.wait_ge(s_y_mm, b)
                    nc.vector.tensor_tensor(hc[:, k, :], state[:, k, :], csb[:, k, :], ALU.mult).then_inc(s_hc, 1)
                if more:
                    layer_norm(b + 1, steps)
                for i in range(KI):
                    dve.wait_ge(s_h2i_mm, KI * b + i + 1)
                    dve.wait_ge(s_z, KI * (b + 1))
                    nc.vector.tensor_tensor(zs[:, i, :], acc[(21 + i) % 4][:, :], zs[:, i, :],
                                            ALU.mult).then_inc(s_gated, 1)
                    if i == 0 and more:
                        evacuate_transposes(b + 1)
                for j in range(TB):
                    dve.wait_ge(s_out_mm, TB * b + j + 1)
                    dve.wait_ge(s_xr, b + 1)
                    slot = x1[:, bass.ds(b * TB + j, 1), :]
                    nc.vector.tensor_tensor(slot, acc[(29 + j) % 4][:, :].rearrange("p (o d) -> p o d", o=1), slot,
                                            ALU.add).then_inc(s_x1, 1)
                return steps.n

            dve.wait_ge(s_nega, 1)
            steps = Steps(dve, s_v)
            nc.vector.tensor_scalar(neg_a[:, :], neg_a[:, :], -1.0, None, ALU.mult).then_inc(s_nega, 1)
            layer_norm(0, steps)
            dve.wait_ge(s_const, 16 * 5)
            evacuate_transposes(0)
            LN0 = steps.n
            PER = 6 + 2 * KI + NS + LN0
            with dve.Fori(0, batches - 1) as b:
                n = mixer(b, True)
            assert n == PER, (n, PER)
            mixer(batches - 1, False)

        @block.scalar
        def _(act):
            def deviations(b):
                act.wait_ge(s_ve, b + 1)
                nc.scalar.activation(std[:, :, :], var_eps[:, :, :], ACT.Sqrt).then_inc(s_std, 1)

            def mixer(b, more):
                act.wait_ge(s_dt_abs, b + 1)
                nc.scalar.activation(dte[:, :], dta[:, :], ACT.Exp).then_inc(s_dt_exp, 1)
                for k in range(4):
                    act.wait_ge(s_bc_mm, 4 * b + k + 1)
                    if k == 0:
                        act.wait_ge(s_hc, NS * b)
                    dst = bsb if k < 2 else csb
                    nc.scalar.activation(dst[:, k % 2, :], acc[(1 + k) % 4][:, :], ACT.Copy).then_inc(s_bc, 1)
                act.wait_ge(s_dt_u, b + 1)
                nc.scalar.activation(dtl[:, :], dtu[:, :], ACT.Ln).then_inc(s_dt_ln, 1)
                act.wait_ge(s_dt, b + 1)
                act.wait_ge(s_nega, 2)
                act.wait_ge(s_spread, NS * b)
                nc.scalar.activation(decay[:, :], dt[:, :], ACT.Exp, scale=neg_a[:, 0:1]).then_inc(s_decay, 1)
                for i in range(KI):
                    act.wait_ge(s_silu, KI * b + max(i - 2, 0))
                    act.wait_ge(s_xi_mm, KI * b + i + 1)
                    nc.scalar.activation(xa[:, i % 3, :], acc[(5 + i) % 4][:, :], ACT.Copy,
                                         scale=convw[:, i, 3:4]).then_inc(s_tap, 1)
                    if i:
                        silu(b, i - 1)
                silu(b, KI - 1)
                for i in range(KI):
                    act.wait_ge(s_z_mm, KI * b + i + 1)
                    if i == 0:
                        act.wait_ge(s_out_mm, TB * b)
                    nc.scalar.activation(zs[:, i, :], acc[(13 + i) % 4][:, :], ACT.Silu).then_inc(s_z, 1)
                    if i == 5 and more:
                        deviations(b + 1)
                act.wait_ge(s_y_mm, b + 1)
                nc.scalar.activation(ysb[:, :], ps_y[0:H, :], ACT.Copy).then_inc(s_y, 1)

            def silu(b, i):
                act.wait_ge(s_conv, KI * b + i + 1)
                act.wait_ge(s_xs_read, KI * b + max(i - 1, 0))
                nc.scalar.activation(xs[:, i % 2, :], xa[:, i % 3, :], ACT.Silu).then_inc(s_silu, 1)

            act.wait_ge(s_const, 16 * 5)
            nc.scalar.activation(neg_a[:, :], alog[:, :], ACT.Exp).then_inc(s_nega, 1)
            deviations(0)
            with act.Fori(0, batches - 1) as b:
                mixer(b, True)
            mixer(batches - 1, False)

        @block.tensor
        def _(pe):
            def transposes(b):
                for j in range(TB):
                    if j == 0:
                        pe.wait_ge(s_hln, b + 1)
                        pe.wait_ge(s_y, b)
                        pe.wait_ge(s_scan, NS * b)
                    if j >= 2:
                        pe.wait_ge(s_xnT, TB * b + j - 1)
                    for k in range(KD):
                        ins = nc.tensor.transpose(tbank[j % 2][:, k * P:(k + 1) * P],
                                                  hn[:, j, k * P:(k + 1) * P], ident[:, :])
                    ins.then_inc(s_tr, 1)

            def project(n, col, width, done):
                for k in range(KD):
                    ins = nc.tensor.matmul(acc[n % 4][0:width, :], win[:, k, col:col + width], xnT[:, k, :],
                                           start=(k == 0), stop=(k == KD - 1))
                ins.then_inc(done, 1)

            def head_means(b, i):
                pe.wait_ge(s_silu, KI * b + i + 1)
                if i == 0:
                    pe.wait_ge(s_gain, b)
                ins = nc.tensor.matmul(ps_mean[0:H, :], head_mean[:, i, :], xs[:, i % 2, :],
                                       start=(i == 0), stop=(i == KI - 1), skip_group_check=True)
                ins.then_inc(s_xs_read, 1)

            def spread_rows(b, k):
                pe.wait_ge(s_gain, b + 1)
                pe.wait_ge(s_decay, b + 1)
                pe.wait_ge(s_scan, NS * b + k)
                pe.wait_ge(s_xnT, TB * (b + 1))
                nc.tensor.matmul(ps_decay[:, :], spread[:, k, :], decay[:, :], start=True, stop=True)
                nc.tensor.matmul(ps_gain[:, :], spread[:, k, :], gain[:, :], start=True,
                                 stop=True).then_inc(s_spread, 1)

            def mixer(b, more):
                pe.wait_ge(s_xnT, TB * (b + 1))
                pe.wait_ge(s_x1, TB * b)
                pe.wait_ge(s_w_in[0], 16)
                project(0, O_DT, H, s_dt_mm)
                for k in range(4):
                    if k == 3:
                        pe.wait_ge(s_v, DT_READ + b * PER)
                    project(1 + k, O_B + k * P, P, s_bc_mm)
                pe.wait_ge(s_w_in[1], 16)
                for i in range(KI):
                    if i < 4:
                        pe.wait_ge(s_bc, 4 * b + i + 1)
                    else:
                        pe.wait_ge(s_conv, KI * b + i - 3)
                    project(5 + i, O_XI + i * P, P, s_xi_mm)
                    if i == 0:
                        pe.wait_ge(s_w_rest, 16 * 6)
                    if i >= 2:
                        head_means(b, i - 2)
                pe.wait_ge(s_w_in[2], 16)
                for i in range(KI):
                    if i < 4:
                        pe.wait_ge(s_conv, KI * b + 5 + i)
                    else:
                        pe.wait_ge(s_z, KI * b + i - 3)
                    project(13 + i, i * P, P, s_z_mm)
                    if i < 2:
                        head_means(b, KI - 2 + i)
                    if i == 3:
                        spread_rows(b, 0)
                    if i == 5:
                        spread_rows(b, 1)
                pe.wait_ge(s_hc, NS * (b + 1))
                for k in range(NS):
                    ins = nc.tensor.matmul(ps_y[0:H, :], state_sum[:, k, :], hc[:, k, :],
                                           start=(k == 0), stop=(k == NS - 1))
                ins.then_inc(s_y_mm, 1)
                pe.wait_ge(s_y, b + 1)
                for i in range(KI):
                    if i < 4:
                        pe.wait_ge(s_z, KI * b + 5 + i)
                    else:
                        pe.wait_ge(s_gated, KI * b + i - 3)
                    nc.tensor.matmul(acc[(21 + i) % 4][:, :], wh2i[:, i * P:(i + 1) * P], ysb[:, :],
                                     start=True, stop=True).then_inc(s_h2i_mm, 1)
                    if i == 1 and more:
                        transposes(b + 1)
                pe.wait_ge(s_gated, KI * (b + 1))
                for j in range(TB):
                    for i in range(KI):
                        ins = nc.tensor.matmul(acc[(29 + j) % 4][:, :], zs[:, i, j * P:(j + 1) * P], wout[:, i, :],
                                               start=(i == 0), stop=(i == KI - 1))
                    ins.then_inc(s_out_mm, 1)

            LN0 = 4
            PER = 6 + 2 * KI + NS + LN0
            DT_READ = LN0 + 1
            pe.wait_ge(s_const, 16 * 5)
            transposes(0)
            with pe.Fori(0, batches - 1) as b:
                mixer(b, True)
            mixer(batches - 1, False)


def attention_phase(nc, dram, x1, ident, identb, batches):
    SEQ = 512
    TB = SEQ // P
    G, R, DH = 8, 4, 16
    D = G * R * DH
    Q_PART = (0, 0, 1, 1, 0, 2)
    K_PART = (0, 1, 0, 1, 2, 0)
    KQ = len(Q_PART) * DH
    KM = KQ + 3
    UNITS = TB * R // 2
    VW = 32
    SCALE = 1.0 / 4.0
    L = G - 1

    with ExitStack() as ctx:
        sb = lambda name, shape, dt=F32: ctx.enter_context(nc.sbuf_tensor(name, shape, dt))
        ps = lambda name, shape, dt=F32: ctx.enter_context(nc.psum_tensor(name, shape, dt))
        sem = lambda name: ctx.enter_context(nc.semaphore(name))

        q = sb("q", [P, TB, D])
        ast = sb("ast", [P, TB, 6])
        amv = sb("amv", [P, TB, 2])
        ave = sb("ave", [P, TB])
        asd = sb("asd", [P, TB])
        ars = sb("ars", [P, TB])
        q_part = [sb(f"q_part{i}", [P, TB, SEQ], BF16) for i in range(3)]
        q_rest = sb("q_rest", [P, TB, SEQ])
        k_part = [sb(f"k_part{i}", [P, SEQ], BF16) for i in range(3)]
        k_rest = sb("k_rest", [P, SEQ])
        keys = sb("keys", [P, TB, G * DH])
        values = sb("values", [P, TB, G, VW])
        q_stack = sb("q_stack", [KM, G * R, SEQ], BF16)
        k_stack = sb("k_stack", [KM, G, SEQ], BF16)
        mx = sb("mx", [P, G, R * TB])
        mneg = sb("mneg", [P, R * TB])
        mrest = sb("mrest", [P, R * TB])
        mpart = sb("mpart", [P, TB, 3 * R], BF16)
        mT = sb("mT", [3 * R, SEQ], BF16)
        prob = sb("prob", [P, UNITS, 2, SEQ])
        oT = sb("oT", [P, SEQ])
        rsum = sb("rsum", [P, TB, R])
        ao = sb("ao", [P, TB, D])

        ps_s = [ps(f"ps_s{i}", [P, 2, SEQ]) for i in range(2)]
        ps_m = [ps(f"ps_m{i}", [P, SEQ]) for i in range(2)]
        ps_o = ps("ps_o", [P, SEQ])
        ps_t = ps("ps_t", [P, SEQ])
        ps_tb = ps_t[0:3 * R, 0:SEQ // 2].bitcast(BF16)
        prep_bank = [ps_t, ps_m[0], ps_m[1], ps_o]

        s_ctx, s_ones, s_zero = sem("context_loaded"), sem("ones_set"), sem("values_zeroed")
        s_val, s_ktr, s_khi, s_krest, s_ksplit = (sem(n) for n in (
            "values_ready", "keys_transposed", "k_high", "k_rest_ready", "k_split"))
        s_ve, s_sd, s_ln = sem("avar_ready"), sem("astd_ready"), sem("q_ready")
        s_qtr, s_qhi, s_qrest, s_qsplit = (sem(n) for n in ("q_transposed", "q_high", "q_rest_ready", "q_split"))
        s_kst, s_qst, s_mrow = sem("k_stacked"), sem("q_stacked"), sem("max_rows_in")
        s_mm, s_max, s_msplit, s_mtr, s_mev = (sem(n) for n in (
            "max_scores", "max_done", "max_split", "max_transposed", "max_copied"))
        s_sc, s_exp, s_pv, s_otc, s_back, s_fin, s_res = (sem(n) for n in (
            "scores", "exp_done", "pv_done", "out_copied", "out_transposed", "group_done", "residual_added"))
        s_v, s_p = sem("avector_steps"), sem("apool_steps")

        block = ctx.enter_context(nc.Block())

        @block.sync
        def _(sp):
            def stack(b):
                sp.wait_ge(s_ktr, TB * b)
                sp.wait_ge(s_val, b)
                alone(sp)
                sp.dma_start(keys[:, :, :], dram["ctx"][bass.ds(b * TB, TB)].rearrange("t p d -> p t d")
                             ).then_inc(s_ctx, 16)
                sp.wait_ge(s_sc, UNITS * G * b)
                alone(sp)
                sp.wait_ge(s_ksplit, b + 1)
                alone(sp)
                for i, part in enumerate(K_PART):
                    for g in range(G):
                        sp.dma_start(k_stack[i * DH:(i + 1) * DH, g, :],
                                     k_part[part][g * DH:(g + 1) * DH, :]).then_inc(s_kst, 16)
                sp.wait_ge(s_qsplit, TB * (b + 1))
                for j in range(P // DH):
                    for i, part in enumerate(Q_PART):
                        sp.dma_start(q_stack[i * DH:(i + 1) * DH, j::P // DH, :],
                                     q_part[part][j * DH:(j + 1) * DH, :, :]).then_inc(s_qst, 16)

            def max_rows(n, g):
                sp.wait_ge(s_mev, n + 1)
                alone(sp)
                for i in range(3):
                    sp.dma_start(q_stack[KQ + i:KQ + i + 1, bass.ds(g * R, R), :],
                                 mT[i * R:(i + 1) * R, :]).then_inc(s_mrow, 16)

            with sp.Fori(0, batches) as b:
                stack(b)
                with sp.Fori(0, G) as g:
                    max_rows(b * G + g, g)

        @block.gpsimd
        def _(pool):
            K_STEPS, Q_STEPS, M_STEPS = 1, 1, 4

            def split(steps, rest, parts, done):
                alone(pool)
                steps.then(nc.gpsimd.tensor_copy(parts[1], rest))
                nc.gpsimd.tensor_tensor(parts[2], rest, parts[1], ALU.subtract).then_inc(done, 1)

            def prepare(b):
                steps = Steps(pool, s_p, b * (1 + TB + G * M_STEPS))
                pool.wait_ge(s_ctx, 16 * (b + 1))
                pool.wait_ge(s_pv, TB * G * b)
                alone(pool)
                nc.gpsimd.tensor_copy(values[:, :, :, 0:DH],
                                      keys[:, :, :].rearrange("p t (g d) -> p t g d", g=G)).then_inc(s_val, 1)
                pool.wait_ge(s_krest, b + 1)
                pool.wait_ge(s_kst, 16 * len(K_PART) * G * b)
                split(steps, k_rest[:, :], [p[:, :] for p in k_part], s_ksplit)
                for c in range(TB):
                    pool.wait_ge(s_qrest, TB * b + c + 1)
                    if c == 0:
                        pool.wait_ge(s_qst, 16 * len(Q_PART) * (P // DH) * b)
                    split(steps, q_rest[:, c, :], [p[:, c, :] for p in q_part], s_qsplit)

            def split_max(b, g):
                steps = Steps(pool, s_p, b * (1 + TB + G * M_STEPS) + 1 + TB + g * M_STEPS)
                n = b * G + g
                pool.wait_ge(s_max, R * TB * (n + 1))
                pool.wait_ge(s_mtr, n)
                alone(pool)
                steps.then(nc.gpsimd.tensor_copy(mrest[:, :].rearrange("p (o k) -> p o k", o=1),
                                                 mx[:, bass.ds(g, 1), :]))
                alone(pool)
                steps.then(nc.gpsimd.tensor_scalar(mneg[:, :], mrest[:, :], -1.0, None, ALU.mult))
                view = lambda t: t.rearrange("p (r t) -> p t r", r=R)
                part = lambda i: mpart[:, :, i * R:(i + 1) * R]
                alone(pool)
                steps.then(nc.gpsimd.tensor_copy(part(0), view(mneg[:, :])))
                steps.then(nc.gpsimd.tensor_tensor(view(mrest[:, :]), view(mneg[:, :]), part(0), ALU.subtract))
                alone(pool)
                nc.gpsimd.tensor_copy(part(1), view(mrest[:, :])).then_inc(s_msplit, 1)
                pool.wait_ge(s_msplit, 2 * n + 1)
                nc.gpsimd.tensor_tensor(part(2), view(mrest[:, :]), part(1), ALU.subtract).then_inc(s_msplit, 1)

            nc.gpsimd.memset(values[:, :, :, :], 0.0).then_inc(s_zero, 1)
            pool.wait_ge(s_zero, 1)
            nc.gpsimd.memset(values[:, :, :, DH:DH + 1], 1.0).then_inc(s_zero, 1)
            pool.wait_ge(s_zero, 2)
            nc.gpsimd.memset(k_stack[KQ:KM, :, :], 1.0).then_inc(s_ones, 1)
            pool.wait_ge(s_ones, 1)
            with pool.Fori(0, batches) as b:
                prepare(b)
                with pool.Fori(0, G) as g:
                    split_max(b, g)
                pool.wait_ge(s_fin, G * (b + 1))
                slot = x1[:, bass.ds(b * TB, TB), :]
                nc.gpsimd.tensor_tensor(slot, slot, ao[:, :, :], ALU.add).then_inc(s_res, 1)

        @block.vector
        def _(dve):
            dve.wait_ge(s_ones, 1)
            PER = 3 + G

            def prepare(b):
                steps = Steps(dve, s_v, b * PER)
                for j in range(TB):
                    ins = nc.vector.bn_stats(ast[:, j, :], x1[:, bass.ds(b * TB + j, 1), :]
                                             .rearrange("p o d -> p (o d)"))
                steps.then(ins)
                alone(dve)
                for j in range(TB):
                    ins = nc.vector.bn_aggr(amv[:, j, :], ast[:, j, :])
                steps.then(ins)
                nc.vector.tensor_scalar(ave[:, :], amv[:, :, 1], LN_EPS, None, ALU.add).then_inc(s_ve, 1)
                dve.wait_ge(s_sd, b + 1)
                steps.then(nc.vector.reciprocal(ars[:, :], asd[:, :]))
                dve.wait_ge(s_qtr, TB * b)
                for j in range(TB):
                    ins = nc.vector.tensor_scalar(q[:, j, :].rearrange("p (o d) -> p o d", o=1),
                                                  x1[:, bass.ds(b * TB + j, 1), :],
                                                  amv[:, j, 0:1], ars[:, j:j + 1], ALU.subtract, ALU.mult)
                ins.then_inc(s_ln, 1)
                dve.wait_ge(s_khi, b + 1)
                dve.wait_ge(s_ksplit, b)
                nc.vector.tensor_tensor(k_rest[:, :], ps_s[0][:, 0, :], k_part[0][:, :],
                                        ALU.subtract).then_inc(s_krest, 1)
                for c in range(TB):
                    dve.wait_ge(s_qhi, TB * b + c + 1)
                    if c == 0:
                        dve.wait_ge(s_qsplit, TB * b)
                    nc.vector.tensor_tensor(q_rest[:, c, :], prep_bank[c][:, :], q_part[0][:, c, :],
                                            ALU.subtract).then_inc(s_qrest, 1)

            def maxima(b, g, u):
                for k in (2 * u, 2 * u + 1):
                    dve.wait_ge(s_mm, R * TB * (b * G + g) + k + 1)
                    if k == 0 :
                        dve.wait_ge(s_msplit, 2 * G * b)
                    nc.vector.tensor_reduce(mx[:, bass.ds(g, 1), k:k + 1], ps_m[k % 2][:, :].rearrange(
                        "p (o d) -> p o d", o=1), AX.X, ALU.max).then_inc(s_max, 1)

            def finish(b, g):
                n = b * G + g
                dve.wait_ge(s_back, n + 1)
                out4 = ps_t[:, :].rearrange("p (t r w) -> p t r w", t=TB, r=R)
                nc.vector.reciprocal(rsum[:, :, :], out4[:, :, :, DH]).then_inc(s_v, 1)
                dve.wait_ge(s_v, b * PER + 3 + g + 1)
                dve.wait_ge(s_res, b)
                nc.vector.tensor_tensor(
                    ao[:, :, bass.ds(g * R * DH, R * DH)].rearrange("p t (r d) -> p t r d", r=R),
                    out4[:, :, :, 0:DH],
                    rsum[:, :, :].rearrange("p t (r o) -> p t r o", o=1).to_broadcast([P, TB, R, DH]),
                    ALU.mult).then_inc(s_fin, 1)

            def group(b, g, do_max, first):
                for u in range(UNITS):
                    if do_max:
                        maxima(b, g + 2, u)
                    if u == 6 and not first:
                        finish(b, g - 1)

            with dve.Fori(0, batches) as b:
                prepare(b)
                for g in (0, 1):
                    for u in range(UNITS):
                        maxima(b, g, u)
                group(b, 0, True, True)
                with dve.Fori(1, L - 1) as g:
                    group(b, g, True, False)
                group(b, L - 1, False, False)
                group(b, L, False, False)
                finish(b, L)

        @block.scalar
        def _(act):
            def prepare(b):
                act.wait_ge(s_ktr, TB * (b + 1))
                act.wait_ge(s_kst, 16 * len(K_PART) * G * b)
                nc.scalar.activation(k_part[0][:, :], ps_s[0][:, 0, :], ACT.Copy).then_inc(s_khi, 1)
                act.wait_ge(s_ve, b + 1)
                nc.scalar.activation(asd[:, :], ave[:, :], ACT.Sqrt).then_inc(s_sd, 1)
                act.wait_ge(s_qst, 16 * len(Q_PART) * (P // DH) * b)
                for c in range(TB):
                    act.wait_ge(s_qtr, TB * b + c + 1)
                    nc.scalar.activation(q_part[0][:, c, :], prep_bank[c][:, :], ACT.Copy).then_inc(s_qhi, 1)

            def copy_max(b, g):
                n = b * G + g
                act.wait_ge(s_mtr, n + 1)
                act.wait_ge(s_mrow, 16 * 3 * n)
                nc.scalar.activation(mT[:, :], ps_tb, ACT.Copy).then_inc(s_mev, 1)

            def copy_out(b, g):
                n = b * G + g
                act.wait_ge(s_pv, TB * (n + 1))
                act.wait_ge(s_back, n)
                nc.scalar.activation(oT[:, :], ps_o[:, :], ACT.Copy).then_inc(s_otc, 1)

            def group(b, g, do_m, first):
                n = b * G + g
                for u in range(UNITS):
                    act.wait_ge(s_sc, UNITS * n + u + 1)
                    act.wait_ge(s_pv, TB * n if first else TB * n - TB + u // 2 + 1)
                    nc.scalar.activation(prob[:, u, :, :], ps_s[u % 2][:, :, :], ACT.Exp,
                                         scale=SCALE).then_inc(s_exp, 1)
                    if u == 2 and not first:
                        copy_out(b, g - 1)
                    if u == 3 and do_m:
                        copy_max(b, g + 1)

            with act.Fori(0, batches) as b:
                prepare(b)
                copy_max(b, 0)
                group(b, 0, True, True)
                with act.Fori(1, L - 1) as g:
                    group(b, g, True, False)
                group(b, L - 1, True, False)
                group(b, L, False, False)
                copy_out(b, L)

        @block.tensor
        def _(pe):
            def prepare(b):
                pe.wait_ge(s_ctx, 16 * (b + 1))
                pe.wait_ge(s_exp, UNITS * G * b)
                for t in range(TB):
                    nc.tensor.transpose(ps_s[0][:, 0, t * P:(t + 1) * P], keys[:, t, :], ident[:, :]
                                        ).then_inc(s_ktr, 1)
                pe.wait_ge(s_ln, b + 1)
                pe.wait_ge(s_fin, G * b)
                pe.wait_ge(s_max, R * TB * G * b)
                for c in range(TB):
                    for t in range(TB):
                        ins = nc.tensor.transpose(prep_bank[c][:, t * P:(t + 1) * P],
                                                  q[:, t, c * P:(c + 1) * P], ident[:, :])
                    ins.then_inc(s_qtr, 1)

            def max_scores(b, g, u, first=False):
                for k in (2 * u, 2 * u + 1):
                    r, t = k // TB, k % TB
                    if not (first and k < 2):
                        pe.wait_ge(s_max, R * TB * (b * G + g) + k - 1)
                    nc.tensor.matmul(ps_m[k % 2][:, :], q_stack[0:KQ, bass.ds(g * R + r, 1), t * P:(t + 1) * P]
                                     .rearrange("p o t -> p (o t)"),
                                     k_stack[0:KQ, bass.ds(g, 1), :].rearrange("p o t -> p (o t)"),
                                     start=True, stop=True).then_inc(s_mm, 1)

            def transpose_max(b, g, first):
                n = b * G + g
                pe.wait_ge(s_msplit, 2 * (n + 1))
                pe.wait_ge(s_fin, G * b if first else n - 2)
                for t in range(TB):
                    ins = nc.tensor.transpose(ps_tb[:, t * P:(t + 1) * P], mpart[:, t, :], identb[:, :])
                ins.then_inc(s_mtr, 1)

            def products(b, g, t):
                n = b * G + g
                pe.wait_ge(s_exp, UNITS * n + 2 * t + 2)
                if t == 0:
                    pe.wait_ge(s_otc, n)
                for r in range(R):
                    ins = nc.tensor.matmul(ps_o[r * VW:(r + 1) * VW, :],
                                           values[:, t, g, :],
                                           prob[:, 2 * t + r // 2, r % 2, :],
                                           start=(t == 0), stop=(t == TB - 1), tile_position=(0, r * VW))
                ins.then_inc(s_pv, 1)

            def transpose_out(b, g, m_copied):
                pe.wait_ge(s_otc, b * G + g + 1)
                pe.wait_ge(s_mev, m_copied)
                pe.wait_ge(s_fin, b * G + g)
                for t in range(TB):
                    ins = nc.tensor.transpose(ps_t[:, t * P:(t + 1) * P], oT[:, t * P:(t + 1) * P], ident[:, :])
                ins.then_inc(s_back, 1)

            def group(b, g, do_max, do_m, first):
                n = b * G + g
                pe.wait_ge(s_mrow, 16 * 3 * (n + 1))
                for u in range(UNITS):
                    t = u // 2
                    pe.wait_ge(s_exp, UNITS * n if first and u < 2 else UNITS * n + u - 1)
                    for i in range(2):
                        r = u % 2 * 2 + i
                        ins = nc.tensor.matmul(ps_s[u % 2][:, i, :],
                                               k_stack[:, bass.ds(g, 1), t * P:(t + 1) * P]
                                               .rearrange("p o t -> p (o t)"),
                                               q_stack[:, bass.ds(g * R + r, 1), :].rearrange("p o t -> p (o t)"),
                                               start=True, stop=True)
                    ins.then_inc(s_sc, 1)
                    if do_max:
                        max_scores(b, g + 2, u)
                    if u == 1 and not first:
                        products(b, g - 1, TB - 1)
                    if u == 2 and do_m:
                        transpose_max(b, g + 1, first)
                    if u in (3, 5, 7):
                        products(b, g, (u - 3) // 2)
                    if u == 5 and not first:
                        transpose_out(b, g - 1, n + 2 if do_m else n + 1)

            pe.wait_ge(s_zero, 2)
            pe.wait_ge(s_ones, 1)
            with pe.Fori(0, batches) as b:
                prepare(b)
                pe.wait_ge(s_qrest, TB * (b + 1))
                pe.wait_ge(s_krest, b + 1)
                pe.wait_ge(s_val, b + 1)
                pe.wait_ge(s_kst, 16 * len(K_PART) * G * (b + 1))
                pe.wait_ge(s_qst, 16 * len(Q_PART) * (P // DH) * (b + 1))
                for g in (0, 1):
                    for u in range(UNITS):
                        max_scores(b, g, u, first=(g == 0))
                transpose_max(b, 0, True)
                group(b, 0, True, True, True)
                for g in range(1, L - 1):
                    group(b, g, True, True, False)
                group(b, L - 1, False, True, False)
                group(b, L, False, False, False)
                products(b, L, TB - 1)
                transpose_out(b, L, G * (b + 1))


def at_least(engine, sem, value):
    if not isinstance(value, int) or value > 0:
        engine.wait_ge(sem, value)


def experts_phase(nc, dram, x1, ident, out):
    TOKENS, D = 2048, 512
    T = TOKENS // P
    KD = D // P
    E = 16
    TOP = 2
    F = 256
    KF = F // P
    TILES = (TOP * TOKENS - E) // P + E
    RING = 4
    B = 4
    WUP = KD * 2 * F
    WCOLS = WUP + KF * D
    list_x, list_y = dram["list_x"], dram["list_y"]

    with ExitStack() as ctx:
        sb = lambda name, shape, dt=F32: ctx.enter_context(nc.sbuf_tensor(name, shape, dt))
        ps = lambda name, shape=(P, 512), dt=F32: ctx.enter_context(nc.psum_tensor(name, list(shape), dt))
        sem = lambda name: ctx.enter_context(nc.semaphore(name))

        xn = sb("xn", [P, T, D])
        xnT = sb("mxnT", [P, KD, TOKENS])
        w_shared = sb("w_shared", [P, WCOLS])
        ring = sb("ring", [P, RING, WCOLS])
        gate_w = sb("gate_w", [P, KD, E])
        bias = sb("bias", [P, 1, E])
        iota_e = sb("iota_e", [P, 1, E])
        iota_j = sb("iota_j", [1, TILES, 1])
        before = sb("before", [P, P], BF16)
        ones = sb("ones", [P, P], BF16)
        restart = sb("restart", [P, E, T])
        mst = sb("mst", [P, T, 6])
        mmv = sb("mmv", [P, T, 2])
        mve = sb("mve", [P, T])
        msd = sb("msd", [P, T])
        mrs = sb("mrs", [P, T])
        score = sb("score", [P, T, E])
        biased = sb("biased", [P, T, E])
        top8 = sb("top8", [P, T, 8])
        idx8 = sb("idx8", [P, T, 8], mybir.dt.uint32)
        idx = sb("idx", [P, TOP, T])
        chosen = sb("chosen", [P, TOP, T, E])
        picked = sb("picked", [P, T, E])
        weight = sb("weight", [P, TOP, T])
        total = sb("total", [P, T])
        assign = sb("assign", [P, E, T], BF16)
        upto = sb("upto", [P, E, T], BF16)
        earlier = sb("earlier", [P, E, T], BF16)
        count = sb("count", [P, E], mybir.dt.int32)
        tiles = sb("tiles", [P, E])
        ends = sb("ends", [P, E])
        onesf = sb("onesf", [P, E])
        first = sb("first", [P, E, 1])
        slots = sb("slots", [P, E, T])
        slotf = sb("slotf", [P, TOP, T])
        slot = sb("slot", [P, TOP, T], mybir.dt.uint32)
        past = sb("past", [1, TILES, E])
        owner = sb("owner", [1, TILES])
        ends_i = sb("ends_i", [1, E], mybir.dt.int32)
        owner_i = sb("owner_i", [1, TILES], mybir.dt.int32)
        slot_i = sb("slot_i", [1, TILES], mybir.dt.int32)
        hS = sb("hS", [P, KF, 512])
        xg = sb("xg", [P, 2, D])
        xgT = sb("xgT", [P, 2, KD * P])
        sg = sb("sg", [P, 2, F])
        sS = sb("sS", [P, KF, 512])
        h = sb("h", [P, 2, F])
        hT = sb("hT", [P, 2, KF * P])
        y = sb("y", [P, 2, D])
        res = sb("res", [P, 2, D])
        FETCH = 6
        fetched = xnT[:, :, :].rearrange("p k (a d) -> p (k a) d", d=D)
        assert TILES % 2 == 1

        ps_x = [ps(f"ps_x{i}") for i in range(2)]
        ps_gu = [ps(f"ps_gu{i}") for i in range(2)]
        ps_h = [ps(f"ps_h{i}") for i in range(2)]
        ps_y = [ps(f"ps_yy{i}") for i in range(2)]
        ps_route = ps_h[1]
        quad = [ps_gu[0], ps_gu[1], ps_x[0], ps_x[1]]

        names = ("mconst", "gatew", "wshared", "wload0", "wload1", "wload2", "wload3", "wready", "mve", "mstd", "xn", "xT",
                 "xTc", "logits", "score", "route_a", "route_mm", "table", "slots", "scattered", "su", "ss", "sh",
                 "sd", "sacc", "xg0", "xg1", "tx", "txc", "gu", "sg", "h", "th", "thc", "dn", "yc", "yst0", "yst1",
                 *(f"fetch{i}" for i in range(6)), "ost0", "ost1", "res", "v", "ones")
        s = {n: sem("e_" + n) for n in names}
        block = ctx.enter_context(nc.Block())

        @block.sync
        def _(sp):
            sp.dma_start(gate_w[:, :, :], dram["gate_w"]).then_inc(s["gatew"], 16)
            for dst, name in ((bias[:, 0, :], "expert_bias"), (iota_e[:, 0, :], "iota_e"), (iota_j[:, :, 0], "iota_j"),
                              (before[:, :], "before"), (restart[:, :, :], "restart")):
                sp.dma_start(dst, dram[name]).then_inc(s["mconst"], 16)
            sp.dma_start(w_shared[:, :], dram["w_shared"]).then_inc(s["wshared"], 16)

            def load(e):
                sp.dma_start(ring[:, e % RING, :], dram["w_experts"][e]).then_inc(s[f"wload{e % RING}"], 16)

            def ready(e):
                sp.wait_ge(s[f"wload{e % RING}"], 16 * (e // RING + 1))
                sp.sem_inc(s["wready"], 1)

            for e in range(RING):
                load(e)
            for e in range(RING):
                ready(e)
            sp.wait_ge(s["table"], 1)
            for e in range(RING, E):
                end = sp.value_load(ends_i[0:1, e - RING:e - RING + 1], min_val=0, max_val=TILES)
                sp.wait_ge(s["dn"], end)
                alone(sp)
                load(e)
                if e > RING:
                    ready(e - 1)
            ready(E - 1)

        @block.gpsimd
        def _(pool):
            nc.gpsimd.memset(ones[:, :], 1.0)
            nc.gpsimd.memset(onesf[:, :], 1.0).then_inc(s["ones"], 1)
            pool.wait_ge(s["slots"], 1)
            pool.wait_ge(s["xn"], T)
            for t in range(T):
                for k in range(TOP):
                    pool.indirect_dma_start(
                        out=list_x[:, :], out_offset=bass.IndirectOffsetOnAxis(ap=slot[:, k, t:t + 1], axis=0),
                        in_=xn[:, t, :], in_offset=None).then_inc(s["scattered"], 16)
            pool.wait_ge(s["scattered"], 16 * TOP * T)

            def load_x(n, p):
                at_least(pool, s["tx"], n - 1)
                pool.dma_start(xg[:, p, :], list_x[bass.ds(n * P, P), :]).then_inc(s[f"xg{p}"], 16)

            load_x(0, 0)
            load_x(1, 1)
            load_x(2, 0)
            with pool.Fori(0, (TILES - 3) // 2) as i:
                load_x(2 * i + 3, 1)
                load_x(2 * i + 4, 0)
            pool.wait_ge(s["yst0"], 16 * ((TILES + 1) // 2))
            pool.wait_ge(s["yst1"], 16 * (TILES // 2))
            for t in range(T):
                if t >= FETCH:
                    pool.wait_ge(s["res"], t - FETCH + 1)
                for k in range(TOP):
                    pool.indirect_dma_start(
                        out=fetched[:, (t % FETCH) * TOP + k, :], out_offset=None, in_=list_y[:, :],
                        in_offset=bass.IndirectOffsetOnAxis(ap=slot[:, k, t:t + 1], axis=0),
                        ).then_inc(s[f"fetch{t % FETCH}"], 16)

        @block.vector
        def _(dve):
            V = Steps(dve, s["v"])
            for t in range(T):
                ins = nc.vector.bn_stats(mst[:, t, :], x1[:, t, :])
            V.then(ins)
            for t in range(T):
                ins = nc.vector.bn_aggr(mmv[:, t, :], mst[:, t, :])
            V.then(ins)
            nc.vector.tensor_scalar(mve[:, :], mmv[:, :, 1], LN_EPS, None, ALU.add).then_inc(s["mve"], 1)
            dve.wait_ge(s["mstd"], 1)
            V.then(nc.vector.reciprocal(mrs[:, :], msd[:, :]))
            for t in range(T):
                nc.vector.tensor_scalar(xn[:, t, :], x1[:, t, :], mmv[:, t, 0:1], mrs[:, t:t + 1],
                                        ALU.subtract, ALU.mult).then_inc(s["xn"], 1)

            dve.wait_ge(s["score"], 1)
            dve.wait_ge(s["mconst"], 16 * 5)
            wide = [P, T, E]
            V.then(nc.vector.tensor_tensor(biased[:, :, :], score[:, :, :], bias[:, :, :].to_broadcast(wide), ALU.add))
            for t in range(T):
                ins = nc.vector.max(top8[:, t, :], biased[:, t, :])
            V.then(ins)
            for t in range(T):
                ins = nc.vector.max_index(idx8[:, t, :], top8[:, t, :], biased[:, t, :])
            V.then(ins)
            V.then(nc.vector.tensor_copy(idx[:, :, :], idx8[:, :, 0:TOP].rearrange("p t k -> p k t")))
            col = lambda a: a.rearrange("p (t o) -> p t o", o=1)
            for k in range(TOP):
                V.then(nc.vector.tensor_tensor(chosen[:, k, :, :], iota_e[:, :, :].to_broadcast(wide),
                                               col(idx[:, k, :]).to_broadcast(wide), ALU.is_equal))
            V.then(nc.vector.tensor_tensor(assign[:, :, :].rearrange("p e t -> p t e"), chosen[:, 0, :, :],
                                           chosen[:, 1, :, :], ALU.add))
            dve.wait_ge(s["ones"], 1)
            flat = lambda a: a.rearrange("p e t -> p (e t)")
            V.then(nc.vector.tensor_tensor_scan(flat(upto[:, :, :]), flat(restart[:, :, :]), flat(assign[:, :, :]), 0.0,
                                                ALU.mult, ALU.add))
            nc.vector.tensor_tensor(earlier[:, :, :], upto[:, :, :], assign[:, :, :], ALU.subtract
                                    ).then_inc(s["route_a"], 1)
            for k in range(TOP):
                V.then(nc.vector.tensor_tensor(picked[:, :, :], chosen[:, k, :, :], score[:, :, :], ALU.mult))
                V.then(nc.vector.tensor_reduce(weight[:, k, :], picked[:, :, :], AX.X, ALU.add))
            V.then(nc.vector.scalar_tensor_tensor(out=total[:, :], in0=weight[:, 0, :], scalar=1e-20,
                                                  in1=weight[:, 1, :], op0=ALU.add, op1=ALU.add))
            V.then(nc.vector.reciprocal(total[:, :], total[:, :]))
            V.then(nc.vector.tensor_tensor(weight[:, :, :], weight[:, :, :], total[:, :].rearrange(
                "p (o t) -> p o t", o=1).to_broadcast([P, TOP, T]), ALU.mult))
            dve.wait_ge(s["route_mm"], 1)
            V.then(nc.vector.tensor_scalar(count[:, :], ps_route[:, E * T:E * T + E], float(P - 1), None, ALU.add))
            V.then(nc.vector.tensor_scalar(count[:, :], count[:, :], 7, None, ALU.logical_shift_right))
            V.then(nc.vector.tensor_copy(tiles[:, :], count[:, :]))
            V.then(nc.vector.tensor_tensor_scan(ends[:, :], onesf[:, :], tiles[:, :], 0.0, ALU.mult, ALU.add))
            V.then(nc.vector.tensor_tensor(first[:, :, 0], ends[:, :], tiles[:, :], ALU.subtract))
            V.then(nc.vector.tensor_scalar(first[:, :, 0], first[:, :, 0], float(P), None, ALU.mult))
            V.then(nc.vector.tensor_tensor(slots[:, :, :], ps_route[:, 0:E * T].rearrange("p (e t) -> p e t", e=E),
                                           first[:, :, :].to_broadcast([P, E, T]), ALU.add))
            for k in range(TOP):
                V.then(nc.vector.tensor_tensor(picked[:, :, :], chosen[:, k, :, :],
                                               slots[:, :, :].rearrange("p e t -> p t e"), ALU.mult))
                V.then(nc.vector.tensor_reduce(slotf[:, k, :], picked[:, :, :], AX.X, ALU.add))
            nc.vector.tensor_copy(slot[:, :, :], slotf[:, :, :]).then_inc(s["slots"], 1)
            jwide = [1, TILES, E]
            V.then(nc.vector.tensor_tensor(past[:, :, :], iota_j[:, :, :].to_broadcast(jwide), ends[0:1, :].rearrange(
                "p (o e) -> p o e", o=1).to_broadcast(jwide), ALU.is_ge))
            V.then(nc.vector.tensor_reduce(owner[:, :], past[:, :, :], AX.X, ALU.add))
            V.then(nc.vector.tensor_scalar(owner_i[:, :], owner[:, :], float(E - 1), None, ALU.min))
            V.then(nc.vector.tensor_scalar(slot_i[:, :], owner_i[:, :], RING - 1, None, ALU.bitwise_and))
            nc.vector.tensor_copy(ends_i[:, :], ends[0:1, :]).then_inc(s["table"], 1)

            for b in range(B):
                for f in range(KF):
                    dve.wait_ge(s["ss"], KF * b + f + 1)
                    at_least(dve, s["sd"], 4 * b)
                    nc.vector.tensor_tensor(hS[:, f, :], quad[2 * f + 1][:, :], sS[:, f, :],
                                            ALU.mult).then_inc(s["sh"], 1)
                for j in range(4):
                    t = 4 * b + j
                    dve.wait_ge(s["sd"], t + 1)
                    nc.vector.tensor_tensor(x1[:, t, :], x1[:, t, :], ps_y[j % 2][:, :], ALU.add).then_inc(s["sacc"], 1)

            def gated(n, p):
                dve.wait_ge(s["sg"], n + 1)
                at_least(dve, s["th"], n - 1)
                nc.vector.tensor_tensor(h[:, p, :], ps_gu[p][:, F:2 * F], sg[:, p, :], ALU.mult).then_inc(s["h"], 1)

            def copy_x(n, p):
                dve.wait_ge(s["tx"], n + 1)
                nc.vector.tensor_copy(xgT[:, p, :], ps_x[p][:, :]).then_inc(s["txc"], 1)

            def body(n, p, last):
                gated(n, p)
                if not last:
                    copy_x(n + 1, 1 - p)

            copy_x(0, 0)
            body(0, 0, False)
            with dve.Fori(0, (TILES - 3) // 2) as i:
                body(2 * i + 1, 1, False)
                body(2 * i + 2, 0, False)
            body(TILES - 2, 1, False)
            body(TILES - 1, 0, True)

            for t in range(T):
                f = (t % FETCH) * TOP
                dve.wait_ge(s[f"fetch{t % FETCH}"], 16 * TOP * (t // FETCH + 1))
                if t >= 2:
                    dve.wait_ge(s[f"ost{t % 2}"], 16 * (t // 2))
                V.then(nc.vector.scalar_tensor_tensor(out=res[:, t % 2, :], in0=fetched[:, f, :],
                                                      scalar=weight[:, 0, t:t + 1], in1=x1[:, t, :],
                                                      op0=ALU.mult, op1=ALU.add))
                nc.vector.scalar_tensor_tensor(out=res[:, t % 2, :], in0=fetched[:, f + 1, :],
                                               scalar=weight[:, 1, t:t + 1], in1=res[:, t % 2, :],
                                               op0=ALU.mult, op1=ALU.add).then_inc(s["res"], 1)

        @block.scalar
        def _(act):
            act.wait_ge(s["mve"], 1)
            nc.scalar.activation(msd[:, :], mve[:, :], ACT.Sqrt).then_inc(s["mstd"], 1)
            for t in range(T):
                act.wait_ge(s["xT"], t + 1)
                nc.scalar.activation(xnT[:, :, t * P:(t + 1) * P], ps_x[t % 2][:, :].rearrange("p (k t) -> p k t", k=KD),
                                     ACT.Copy).then_inc(s["xTc"], 1)
            act.wait_ge(s["logits"], T)
            nc.scalar.activation(score[:, :, :], ps_route[:, 0:T * E].rearrange("p (t e) -> p t e", t=T),
                                 ACT.Sigmoid).then_inc(s["score"], 1)
            for b in range(B):
                for f in range(KF):
                    act.wait_ge(s["su"], KF * b + f + 1)
                    at_least(act, s["sh"], KF * b)
                    nc.scalar.activation(sS[:, f, :], quad[2 * f][:, :], ACT.Silu).then_inc(s["ss"], 1)

            def silu(n, p):
                act.wait_ge(s["gu"], n + 1)
                at_least(act, s["h"], n - 1)
                nc.scalar.activation(sg[:, p, :], ps_gu[p][:, 0:F], ACT.Silu).then_inc(s["sg"], 1)

            def copy_h(n, p):
                act.wait_ge(s["th"], n + 1)
                at_least(act, s["dn"], n - 1)
                nc.scalar.activation(hT[:, p, :], ps_h[p][:, 0:KF * P], ACT.Copy).then_inc(s["thc"], 1)

            def copy_y(n, p):
                act.wait_ge(s["dn"], n + 1)
                at_least(act, s[f"yst{p}"], 8 * n - 8 * p)
                nc.scalar.activation(y[:, p, :], ps_y[p][:, :], ACT.Copy).then_inc(s["yc"], 1)

            def store(n, p):
                act.wait_ge(s["yc"], n + 1)
                act.dma_start(list_y[bass.ds(n * P, P), :], y[:, p, :]).then_inc(s[f"yst{p}"], 16)

            def body(n, p):
                silu(n, p)
                if not isinstance(n, int) or n > 1:
                    store(n - 2, p)
                copy_h(n - 1, 1 - p)
                copy_y(n - 1, 1 - p)

            silu(0, 0)
            body(1, 1)
            body(2, 0)
            with act.Fori(0, (TILES - 3) // 2) as i:
                body(2 * i + 3, 1)
                body(2 * i + 4, 0)
            last = TILES - 1
            store(last - 1, 1)
            copy_h(last, 0)
            copy_y(last, 0)
            store(last, 0)
            for t in range(T):
                act.wait_ge(s["res"], t + 1)
                act.dma_start(out[t * P:(t + 1) * P, :], res[:, t % 2, :]).then_inc(s[f"ost{t % 2}"], 16)
            for p in range(2):
                act.wait_ge(s[f"ost{p}"], 16 * (T // 2))

        @block.tensor
        def _(pe):
            pe.wait_ge(s["gatew"], 16)
            for t in range(T + 1):
                if t < T:
                    pe.wait_ge(s["xn"], t + 1)
                    if t >= 2:
                        pe.wait_ge(s["xTc"], t - 1)
                    for k in range(KD):
                        ins = nc.tensor.transpose(ps_x[t % 2][:, k * P:(k + 1) * P], xn[:, t, k * P:(k + 1) * P],
                                                  ident[:, :])
                    ins.then_inc(s["xT"], 1)
                if t:
                    pe.wait_ge(s["xTc"], t)
                    for k in range(KD):
                        ins = nc.tensor.matmul(ps_route[:, (t - 1) * E:t * E], xnT[:, k, (t - 1) * P:t * P],
                                               gate_w[:, k, :], start=(k == 0), stop=(k == KD - 1))
                    ins.then_inc(s["logits"], 1)

            def shared(b):
                cols = slice(b * 512, (b + 1) * 512)
                at_least(pe, s["sh"], KF * b)
                for f in range(KF):
                    for half in range(2):
                        for k in range(KD):
                            c = k * 2 * F + half * F + f * P
                            ins = nc.tensor.matmul(quad[2 * f + half][:, :], w_shared[:, c:c + P], xnT[:, k, cols],
                                                   start=(k == 0), stop=(k == KD - 1))
                    ins.then_inc(s["su"], 1)

            def shared_down(b):
                pe.wait_ge(s["sh"], KF * (b + 1))
                for j in range(4):
                    at_least(pe, s["sacc"], 4 * b + j - 1)
                    for f in range(KF):
                        ins = nc.tensor.matmul(ps_y[j % 2][:, :], hS[:, f, j * P:(j + 1) * P],
                                               w_shared[:, WUP + f * D:WUP + (f + 1) * D],
                                               start=(f == 0), stop=(f == KF - 1))
                    ins.then_inc(s["sd"], 1)

            def ranks():
                pe.wait_ge(s["route_a"], 1)
                pe.wait_ge(s["mconst"], 16 * 5)
                flat = lambda a: a.rearrange("p e t -> p (e t)")
                nc.tensor.matmul(ps_route[:, 0:E * T], before[:, :], flat(assign[:, :, :]), start=True, stop=False)
                nc.tensor.matmul(ps_route[:, 0:E * T], ones[:, :], flat(earlier[:, :, :]), start=False, stop=True)
                nc.tensor.matmul(ps_route[:, E * T:E * T + E], ones[:, :], upto[:, :, T - 1], start=True,
                                 stop=True).then_inc(s["route_mm"], 1)

            pe.wait_ge(s["wshared"], 16)
            shared(0)
            ranks()
            shared_down(0)
            for b in range(1, B):
                shared(b)
                shared_down(b)

            def transpose_x(n, p):
                pe.wait_ge(s[f"xg{p}"], 8 * n + 16 - 8 * p)
                at_least(pe, s["txc"], n - 1)
                for k in range(KD):
                    ins = nc.tensor.transpose(ps_x[p][:, k * P:(k + 1) * P], xg[:, p, k * P:(k + 1) * P], ident[:, :])
                ins.then_inc(s["tx"], 1)

            def gate_up(n, p):
                e = pe.value_load(owner_i[0:1, bass.ds(n, 1)], min_val=0, max_val=E - 1)
                slot = pe.value_load(slot_i[0:1, bass.ds(n, 1)], min_val=0, max_val=RING - 1)
                pe.wait_ge(s["wready"], e + 1)
                pe.wait_ge(s["txc"], n + 1)
                at_least(pe, s["h"], n - 1)
                w = ring[:, bass.ds(slot, 1), :].rearrange("p o c -> p (o c)")
                for k in range(KD):
                    ins = nc.tensor.matmul(ps_gu[p][:, :], xgT[:, p, k * P:(k + 1) * P],
                                           w[:, k * 2 * F:(k + 1) * 2 * F], start=(k == 0), stop=(k == KD - 1))
                ins.then_inc(s["gu"], 1)
                return w

            def transpose_h(n, p):
                pe.wait_ge(s["h"], n + 1)
                at_least(pe, s["thc"], n - 1)
                for k in range(KF):
                    ins = nc.tensor.transpose(ps_h[p][:, k * P:(k + 1) * P], h[:, p, k * P:(k + 1) * P], ident[:, :])
                ins.then_inc(s["th"], 1)

            def down(n, p):
                slot = pe.value_load(slot_i[0:1, bass.ds(n, 1)], min_val=0, max_val=RING - 1)
                w = ring[:, bass.ds(slot, 1), :].rearrange("p o c -> p (o c)")
                pe.wait_ge(s["thc"], n + 1)
                at_least(pe, s["yc"], n - 1)
                for k in range(KF):
                    ins = nc.tensor.matmul(ps_y[p][:, :], hT[:, p, k * P:(k + 1) * P],
                                           w[:, WUP + k * D:WUP + (k + 1) * D], start=(k == 0), stop=(k == KF - 1))
                ins.then_inc(s["dn"], 1)

            def body(n, p, last=False):
                gate_up(n, p)
                if not last:
                    transpose_x(n + 1, 1 - p)
                transpose_h(n - 1, 1 - p)
                down(n - 1, 1 - p)

            pe.wait_ge(s["table"], 1)
            pe.wait_ge(s["sacc"], T)
            transpose_x(0, 0)
            gate_up(0, 0)
            transpose_x(1, 1)
            body(1, 1)
            body(2, 0)
            with pe.Fori(0, (TILES - 5) // 2) as i:
                body(2 * i + 3, 1)
                body(2 * i + 4, 0)
            body(TILES - 2, 1)
            body(TILES - 1, 0, last=True)
            transpose_h(TILES - 1, 0)
            down(TILES - 1, 0)


def build(nc, dram, out):
    rows = 47 * P
    dram["list_x"] = nc.dram_tensor("list_x", (rows, 512), F32, kind="Internal").ap()
    dram["list_y"] = nc.dram_tensor("list_y", (rows, 512), F32, kind="Internal").ap()
    with (
        nc.sbuf_tensor("x1", [P, 16, 512], F32) as x1,
        nc.sbuf_tensor("ident", [P, P], F32) as ident,
        nc.sbuf_tensor("identb", [P, P], BF16) as identb,
    ):
        mixer_phase(nc, dram, x1, ident, identb, 4)
        attention_phase(nc, dram, x1, ident, identb, 4)
        experts_phase(nc, dram, x1, ident, out)


def blocks(a, width=128):
    return np.ascontiguousarray(a.reshape(a.shape[0] // width, width, *a.shape[1:]).swapaxes(0, 1))


def constants():
    f = np.float32
    p = np.arange(128)
    k8, k2, h = np.arange(8), np.arange(2), np.arange(16)
    head_mean = (h[None, None, :] == 2 * k8[None, :, None] + p[:, None, None] // 64).astype(f) / f(64)
    state_sum = (h[None, None, :] == 8 * k2[None, :, None] + p[:, None, None] // 16).astype(f)
    eye = np.eye(128, dtype=f)
    bf = mybir.dt.np(mybir.dt.bfloat16)
    return {
        "ident": eye,
        "identb": eye.astype(bf),
        "head_mean": head_mean,
        "spread": np.ascontiguousarray(state_sum.transpose(2, 1, 0)),
        "state_sum": state_sum,
        "iota_e": np.broadcast_to(np.arange(16, dtype=f), (128, 16)).copy(),
        "iota_j": np.arange(47, dtype=f)[None, :],
        "before": (p[:, None] < p[None, :]).astype(bf),
        "restart": np.broadcast_to((np.arange(16) > 0).astype(f), (128, 16, 16)).copy(),
    }


def layout(i):
    up = np.concatenate([i["L0_ffn_shared_gate_w"], i["L0_ffn_shared_up_w"]], axis=1)
    flat = lambda a: blocks(a).reshape(128, -1)
    return {
        "x": i["x"].reshape(16, 128, 512),
        "ctx": i["ctx_512"].reshape(16, 128, 128),
        "w_in": blocks(i["L0_attn_W_in"].T),
        "w_out": blocks(i["L0_attn_W_out"].T),
        "w_h2i": i["L0_attn_W_h2i"].T,
        "conv": blocks(i["L0_attn_w_conv"][:, 0, :]),
        "w_norm": i["L0_attn_w_norm"].reshape(4, 128).T,
        "dt_bias": i["L0_attn_dt_bias"][:, None],
        "a_log": i["L0_attn_A_log"][:, None],
        "gate_w": blocks(i["L0_ffn_gate_w"]),
        "expert_bias": np.broadcast_to(i["L0_ffn_expert_bias"], (128, 16)),
        "w_shared": np.concatenate([flat(up), flat(i["L0_ffn_shared_down_w"])], axis=1),
        "w_experts": np.stack([np.concatenate([flat(a), flat(b)], axis=1) for a, b in
                               zip(i["L0_ffn_experts_gate_up"], i["L0_ffn_experts_down"])]),
    }


def kernel(**inputs):
    import concourse.bacc as _bacc
    from concourse.bass_utils import run_bass_kernel_spmd as _run

    nc = _bacc.Bacc("TRN2", target_bir_lowering=False, num_devices=1)
    data = layout({k: np.asarray(v) for k, v in inputs.items()}) | constants()
    arrays, dram = {}, {}
    for name, a in data.items():
        a = np.ascontiguousarray(a)
        arrays[f"in_{name}"] = a
        dram[name] = nc.dram_tensor(f"in_{name}", a.shape, mybir.dt.from_np(a.dtype), kind="ExternalInput").ap()
    out = nc.dram_tensor("out", (2048, 512), F32, kind="ExternalOutput").ap()
    build(nc, dram, out)
    r = _run(nc, [arrays], core_ids=[0])
    return r.results[0]["out"].reshape(4, 512, 512)
```
